# Optimizing a Trainium2 kernel written in Bass

```python
import numpy as np
import jax
import jax.numpy as jnp

def _softmax(x, axis=-1):
    return jax.nn.softmax(x, axis=axis)

def _gelu(x):
    return jax.nn.gelu(x, approximate=True)

def _silu(x):
    return jax.nn.silu(x)

def _sigmoid(x):
    return jax.nn.sigmoid(x)

def _layernorm(x, axis=-1, eps=1e-05):
    m = jnp.mean(x, axis=axis, keepdims=True)
    v = jnp.var(x, axis=axis, keepdims=True)
    return (x - m) / jnp.sqrt(v + eps)

def _scatter_add(tgt, idx, src, axis=0):
    return tgt.at[idx].add(src)

def _segment_sum(src, seg, n):
    return jax.ops.segment_sum(src, seg, n)
kernel_name = 'mk_adj_preln_d1_adj_r2_12aef9'

def setup_inputs(seed: int=0):
    np.random.seed(seed)
    _w = jnp.asarray

    def _rec_inputs():
        import jax
        import jax.numpy as jnp
        _gk = jax.random.key(seed)
        x = -0.0002928 + 1 * jax.random.normal(jax.random.fold_in(_gk, 1), (4096, 256), jnp.float32)
        _a = jax.random.bernoulli(jax.random.fold_in(_gk, 2), 0.000488281, (4096, 4096))
        _a = jnp.logical_or(_a, jnp.eye(4096, dtype=bool))
        _af = _a.astype(jnp.float32)
        _af = _af * jax.random.uniform(jax.random.fold_in(_gk, 3), (4096, 4096), jnp.float32, 0.05, 1)
        adj = _af
        return (x, adj)
    x, adj = _rec_inputs()

    def _L0_gnn_setup():
        import jax, jax.numpy as jnp
        import numpy as np
        N = 4096
        IN_F = 256
        NFEAT = 256
        OUT_F = 256
        key = jax.random.key(seed)
        k1, k2, k3, k4, k5 = jax.random.split(key, 5)
        stdv = 1.0 / np.sqrt(OUT_F)
        return {'input': jax.random.normal(k1, (N, IN_F), dtype=jnp.float32), 'adj': jax.random.uniform(k2, (N, N), dtype=jnp.float32), 'x': jax.random.normal(k3, (N, NFEAT), dtype=jnp.float32), 'weight': jax.random.uniform(k4, (IN_F + N + NFEAT, OUT_F), minval=-stdv, maxval=stdv, dtype=jnp.float32), 'bias': jax.random.uniform(k5, (OUT_F,), minval=-stdv, maxval=stdv, dtype=jnp.float32)}
    _L0_gnn_all = _L0_gnn_setup()
    _L0_gnn_in = {k: v for k, v in _L0_gnn_all.items() if k in ('x', 'weight', 'bias')}
    del _L0_gnn_all
    return {'x': x, 'adj': adj, 'L0_gnn_x': _L0_gnn_in['x'], 'L0_gnn_weight': _L0_gnn_in['weight'], 'L0_gnn_bias': _L0_gnn_in['bias']}

def reference(x, adj, L0_gnn_x, L0_gnn_weight, L0_gnn_bias):
    import jax
    import jax.numpy as jnp

    def _L0_gnn_ref(input, adj, x, weight, bias):
        import jax, jax.numpy as jnp
        import numpy as np
        N = 4096
        IN_F = 256
        NFEAT = 256
        OUT_F = 256
        support = jnp.concatenate((adj @ input, adj, x), axis=1)
        return support @ weight + bias
    h = jnp.maximum(_layernorm(x, axis=-1), 0.0)
    x = x + _L0_gnn_ref(h, adj, L0_gnn_x, L0_gnn_weight, L0_gnn_bias)
    return x

_drawn_inputs = setup_inputs


def setup_inputs(seed=0):
    import zlib

    import numpy as np

    out = dict(_drawn_inputs(seed))
    spreads = {}
    factors = {}
    for name, (base, spread) in spreads.items():
        noise = np.random.default_rng([zlib.crc32(name.encode()), seed]).standard_normal(out[name].shape)
        drawn = base * np.exp(spread * noise) if base else spread * noise
        out[name] = jnp.asarray(drawn.astype(out[name].dtype))
    for name, factor in factors.items():
        out[name] = (out[name] * factor).astype(out[name].dtype)
    return out
```

```python
import concourse.bass as bass
from concourse import mybir
from contextlib import ExitStack


P = 128
N = 4096
F = 256
FC = F // P
KT = N // P
TPC = 2
CHUNKS = KT // TPC
TPG = 4
ROWS = TPG * P
GROUPS = N // ROWS
RING = 4
ITER = CHUNKS // RING
EPS = 1e-5
assert ITER == TPG


def build(nc, x, adj, xg, w1, w2, w3, bias, out):
    f32 = mybir.dt.float32
    f32r = mybir.dt.float32r
    ALU = mybir.AluOpType
    ACT = mybir.ActivationFunctionType

    ctx = ExitStack()
    with ctx:
        def sb(name, shape, dt=f32):
            return ctx.enter_context(nc.sbuf_tensor(name, shape, dt))

        def sem(name):
            return ctx.enter_context(nc.semaphore(name))

        V = sb("V", [P, KT + FC, 2, F], f32r)
        X = sb("X", [P, KT, F])
        raw = sb("raw", [P, RING, TPC, ROWS])
        aH = sb("aH", [P, RING, TPC, ROWS], f32r)
        aL = sb("aL", [P, RING, TPC, ROWS], f32r)
        xgraw = sb("xgraw", [P, FC, ROWS])
        xgH = sb("xgH", [P, FC, ROWS], f32r)
        xgL = sb("xgL", [P, FC, ROWS], f32r)
        w2s = sb("w2s", [P, RING, TPC, F])
        w1raw = sb("w1raw", [P, FC, F])
        w3raw = sb("w3raw", [P, FC, F])
        w1H = sb("w1H", [P, FC, F], f32r)
        w1L = sb("w1L", [P, FC, F], f32r)
        bias_all = sb("bias_all", [P, F])
        ident = sb("ident", [P, P])
        eps = sb("eps", [P, 1])
        bn = sb("bn", [P, 2, TPC, 6])
        mv = sb("mv", [P, 2, TPC, 2])
        sd = sb("sd", [P, 2, TPC])
        r0 = sb("r0", [P, 2, TPC])
        nwt = sb("nwt", [P, 2, 5, TPC])
        rstd = sb("rstd", [P, 2, TPC])
        nmr = sb("nmr", [P, 2, TPC])
        xn = sb("xn", [P, 2, TPC, F])
        hH = sb("hH", [P, 2, FC, TPC * P], f32r)
        hL = sb("hL", [P, 2, FC, TPC * P], f32r)
        vf = sb("vf", [P, 2, TPC, F])
        outs = sb("outs", [P, TPG, F])

        acc = ctx.enter_context(nc.psum_tensor("acc", [P, 2 * TPG, 2, F], f32))
        hT = [acc[:, 4 + b, :, :] for b in range(2)]
        vP = [acc[:, 6 + b, :, :] for b in range(2)]

        w1_loaded, w3_loaded = sem("w1_loaded"), sem("w3_loaded")
        bias_loaded = sem("bias_loaded")
        x_first = [sem(f"x_first{i}") for i in range(RING)]
        x_loaded = [sem(f"x_loaded{i}") for i in range(RING)]
        w2_loaded = [sem(f"w2_loaded{i}") for i in range(RING)]
        adj_loaded = [sem(f"adj_loaded{i}") for i in range(RING)]
        xg_loaded = sem("xg_loaded")
        ident_zero, ident_ready, eps_ready = sem("ident_zero"), sem("ident_ready"), sem("eps_ready")
        bn_ready, mv_ready = sem("bn_ready"), sem("mv_ready")
        sd_ready, r0_ready = sem("sd_ready"), sem("r0_ready")
        newton, rstd_ready = sem("newton"), sem("rstd_ready")
        xn_ready, hT_ready = sem("xn_ready"), sem("hT_ready")
        hH_ready, h_ready = sem("hH_ready"), sem("h_ready")
        vP_ready, vf_ready = sem("vP_ready"), sem("vf_ready")
        vH_ready, v_ready = sem("vH_ready"), sem("v_ready")
        w1H_ready, w1_ready = sem("w1H_ready"), sem("w1_ready")
        w3H_ready, w3_ready = sem("w3H_ready"), sem("w3_ready")
        xgH_ready, xg_ready, xg_used = sem("xgH_ready"), sem("xg_ready"), sem("xg_used")
        aH_ready, a_ready = sem("aH_ready"), sem("a_ready")
        tile_summed = sem("tile_summed")
        biased, half_added, evacuated = sem("biased"), sem("half_added"), sem("evacuated")
        out_stored, tail_stored = sem("out_stored"), sem("tail_stored")

        block = ctx.enter_context(nc.Block())

        def inside(i, last):
            return not isinstance(i, int) or 0 <= i < last

        def later(i, first):
            return not isinstance(i, int) or i >= first

        def at(i, step):
            return isinstance(i, int) and i == step

        def chunk_load(n, slot):
            return (n + (RING - slot)) * (16 // RING)

        LEAD = 4

        def steps(eng, step):
            for t in range(-LEAD, 0):
                step(t, t % RING)
            with eng.Fori(0, ITER - 1) as i:
                for u in range(RING):
                    step(i * RING + u, u)
            for t in range(CHUNKS - RING, CHUNKS):
                step(t, t % RING)

        def groups(eng, group):
            group(1, 1)
            with eng.Fori(0, (GROUPS - 2) // 2) as pair:
                group(pair * 2 + 2, 0)
                group(pair * 2 + 3, 1)

        @block.sync
        def _(sp):
            def load_adj(g, c, slot):
                sp.dma_start(raw[:, slot], adj[g, c]).then_inc(adj_loaded[slot], 16)

            def load_w2(s, slot):
                sp.dma_start(w2s[:, slot], w2[:, bass.ds(s * TPC, TPC), :]).then_inc(w2_loaded[slot], 16)

            sp.dma_start(X[:, 0:TPC, :], x[:, 0:TPC, :]).then_inc(x_first[0], 16)
            sp.dma_start(xgraw[:], xg[0]).then_inc(xg_loaded, 16)
            for s in range(RING):
                load_w2(s, s)
                load_adj(0, s, s)
            with sp.Fori(1, ITER) as i:
                for u in range(RING):
                    c = i * RING + u
                    sp.wait_ge(vf_ready, c - (RING - 1))
                    load_w2(c, u)
                    sp.wait_ge(a_ready, c - (RING - 1))
                    load_adj(0, c, u)
            with sp.Fori(1, GROUPS) as g:
                sp.wait_ge(xg_ready, g)
                sp.dma_start(xgraw[:], xg[g]).then_inc(xg_loaded, 16)
                with sp.Fori(0, ITER) as i:
                    for u in range(RING):
                        sp.wait_ge(a_ready, g * CHUNKS + i * RING + (u - (RING - 1)))
                        load_adj(g, i * RING + u, u)
            for j in range(TPG):
                sp.wait_ge(evacuated, (GROUPS - 1) * TPG + j + 1)
                sp.dma_start(out[GROUPS - 1, :, j, :], outs[:, j, :]).then_inc(tail_stored, 16)
            sp.wait_ge(tail_stored, 16 * TPG)

        @block.gpsimd
        def _(pool):
            nc.gpsimd.memset(ident[:], 0.0).then_inc(ident_zero, 1)
            nc.gpsimd.memset(eps[:], EPS).then_inc(eps_ready, 1)
            pool.wait_ge(ident_zero, 1)
            nc.gpsimd.affine_select(out=ident[:], in_=ident[:], compare_op=ALU.not_equal, fill=1.0, base=0,
                                    pattern=[[-1, P]], channel_multiplier=1).then_inc(ident_ready, 1)

            def step(t, u):
                s = t + LEAD
                b = u % 2
                if not inside(s, CHUNKS):
                    return
                var, mean = mv[:, b, :, 1], mv[:, b, :, 0]
                half, r15, negmean, sq, cube = (nwt[:, b, k, :] for k in range(5))
                r = r0[:, b]
                pool.wait_ge(r0_ready, s + 1)
                if later(s, 2):
                    pool.wait_ge(xn_ready, s - 1)
                nc.gpsimd.tensor_tensor(sq, r, r, ALU.mult).then_inc(newton, 1)
                nc.gpsimd.tensor_scalar(half, var, EPS, -0.5, ALU.add, ALU.mult).then_inc(newton, 1)
                nc.gpsimd.tensor_scalar(r15, r, 1.5, 1.0, ALU.mult, ALU.mult).then_inc(newton, 1)
                nc.gpsimd.tensor_scalar(negmean, mean, -1.0, 1.0, ALU.mult, ALU.mult).then_inc(newton, 1)
                pool.wait_ge(newton, s * 7 + 4)
                nc.gpsimd.tensor_tensor(sq, sq, half, ALU.mult).then_inc(newton, 1)
                pool.wait_ge(newton, s * 7 + 5)
                nc.gpsimd.tensor_tensor(cube, sq, r, ALU.mult).then_inc(newton, 1)
                pool.wait_ge(newton, s * 7 + 6)
                nc.gpsimd.tensor_tensor(rstd[:, b], cube, r15, ALU.add).then_inc(newton, 1)
                pool.wait_ge(newton, s * 7 + 7)
                nc.gpsimd.tensor_tensor(nmr[:, b], negmean, rstd[:, b], ALU.mult).then_inc(rstd_ready, 1)
                if inside(s + RING, CHUNKS):
                    load_x(s + RING, u)

            def load_x(s, slot):
                pool.dma_start(X[:, bass.ds(s * TPC, TPC), :], x[:, bass.ds(s * TPC, TPC), :])\
                    .then_inc(x_loaded[slot], 16)

            for t in range(-LEAD, 0):
                step(t, t % RING)
            with pool.Fori(0, ITER - 2) as i:
                for u in range(RING):
                    step(i * RING + u, u)
            for t in range(CHUNKS - 2 * RING, CHUNKS - RING):
                step(t, t % RING)

            pool.wait_ge(xn_ready, CHUNKS)
            pool.wait_ge(bias_loaded, 16)
            with pool.Fori(0, GROUPS - 1) as g:
                with pool.Fori(0, TPG) as j:
                    tile = X[:, bass.ds(g * TPG + j, 1), :]
                    nc.gpsimd.tensor_tensor(tile, tile, bias_all[:].rearrange("p (a f) -> p a f", a=1),
                                            ALU.add).then_inc(biased, 1)
                pool.wait_ge(evacuated, g * TPG + TPG)
                pool.dma_start(out[g], outs[:]).then_inc(out_stored, 16)
                
            for j in range(TPG):
                tile = X[:, (GROUPS - 1) * TPG + j, :]
                nc.gpsimd.tensor_tensor(tile, tile, bias_all[:], ALU.add).then_inc(biased, 1)
            pool.wait_ge(out_stored, 16 * (GROUPS - 1))

        @block.scalar
        def _(act):
            act.dma_start(w1raw[:], w1).then_inc(w1_loaded, 16)
            for s in range(1, RING):
                act.dma_start(X[:, s * TPC:(s + 1) * TPC, :], x[:, s * TPC:(s + 1) * TPC, :])\
                    .then_inc(x_first[s], 16)
            act.dma_start(w3raw[:], w3).then_inc(w3_loaded, 16)
            act.dma_start(bias_all[:], bias.to_broadcast([P, F])).then_inc(bias_loaded, 16)

            def split_high(n, slot):
                act.wait_ge(adj_loaded[slot], chunk_load(n, slot))
                act.wait_ge(tile_summed, n * TPG + TPG)
                nc.scalar.activation(aH[:, slot], raw[:, slot], ACT.Copy).then_inc(aH_ready, 1)

            def split_xg_high(g):
                act.wait_ge(xg_loaded, g * 16 + 16)
                if later(g, 1):
                    act.wait_ge(xg_used, g)
                nc.scalar.activation(xgH[:], xgraw[:], ACT.Copy).then_inc(xgH_ready, 1)

            def step(t, u):
                if at(t, -3):
                    act.wait_ge(w1_loaded, 16)
                    nc.scalar.activation(w1H[:], w1raw[:], ACT.Copy).then_inc(w1H_ready, 1)
                    act.wait_ge(w3_loaded, 16)
                    nc.scalar.activation(V[:, KT:KT + FC, 0, :], w3raw[:], ACT.Copy).then_inc(w3H_ready, 1)
                if inside(t + 2, CHUNKS):
                    s, b = t + 2, u % 2
                    act.wait_ge(hT_ready, s + 1)
                    if later(s, 2):
                        act.wait_ge(vP_ready, s - 1)
                    nc.scalar.activation(hH[:, b], hT[b], ACT.Relu).then_inc(hH_ready, 1)
                if inside(t + 1, CHUNKS):
                    s, b = t + 1, (u + 1) % 2
                    act.wait_ge(vf_ready, s + 1)
                    nc.scalar.activation(V[:, bass.ds(s * TPC, TPC), 0, :], vf[:, b], ACT.Copy)\
                        .then_inc(vH_ready, 1)
                if at(t, -3):
                    split_xg_high(0)
                if inside(t + 3, CHUNKS):
                    split_high(t + 3, (u + 3) % RING)
                if inside(t + 3, CHUNKS):
                    s, b = t + 3, (u + 3) % 2
                    act.wait_ge(rstd_ready, s + 1)
                    if later(s, 2):
                        act.wait_ge(hT_ready, s - 1)
                    for k in range(TPC):
                        last = nc.scalar.activation(xn[:, b, k, :], X[:, bass.ds(s * TPC + k, 1), :], ACT.Identity,
                                                    bias=nmr[:, b, k:k + 1], scale=rstd[:, b, k:k + 1])
                    last.then_inc(xn_ready, 1)
                if inside(t + LEAD, CHUNKS):
                    s, b = t + LEAD, u % 2
                    act.wait_ge(mv_ready, s + 1)
                    if later(s, 2):
                        act.wait_ge(r0_ready, s - 1)
                    nc.scalar.activation(sd[:, b], mv[:, b, :, 1], ACT.Sqrt, bias=eps[:]).then_inc(sd_ready, 1)

            def group(g, par):
                split_xg_high(g)
                with act.Fori(0, ITER) as i:
                    for u in range(RING):
                        split_high(g * CHUNKS + i * RING + u, u)

            act.wait_ge(eps_ready, 1)
            steps(act, step)
            groups(act, group)

        @block.vector
        def _(dve):
            nc.vector.memset(outs[:], 0.0).then_inc(tile_summed, RING * TPG)

            def split_low(n, slot):
                dve.wait_ge(aH_ready, n + 1)
                nc.vector.tensor_tensor(aL[:, slot], raw[:, slot], aH[:, slot].bitcast(f32), ALU.subtract)\
                    .then_inc(a_ready, 1)

            def split_xg_low(g):
                dve.wait_ge(xgH_ready, g + 1)
                nc.vector.tensor_tensor(xgL[:], xgraw[:], xgH[:].bitcast(f32), ALU.subtract).then_inc(xg_ready, 1)

            def evacuate(e, par, j):
                tile = X[:, bass.ds(e * TPG + j, 1), :]
                o = outs[:, bass.ds(j, 1), :]
                if later(e, 1):
                    dve.wait_ge(out_stored, e * 16)
                dve.wait_ge(biased, e * TPG + j + 1)
                dve.wait_ge(tile_summed, e * (CHUNKS * TPG) + ((RING + CHUNKS - 1) * TPG + 1) + j)
                nc.vector.tensor_tensor(o, acc[:, bass.ds(par * TPG + j, 1), 1, :], tile, ALU.add)\
                    .then_inc(half_added, 1)
                dve.wait_ge(half_added, e * TPG + j + 1)
                nc.vector.tensor_tensor(o, acc[:, bass.ds(par * TPG + j, 1), 0, :], o, ALU.add)\
                    .then_inc(evacuated, 1)

            def step(t, u):
                if inside(t + LEAD, CHUNKS):
                    s, b = t + LEAD, u % 2
                    if later(s, 2):
                        dve.wait_ge(rstd_ready, s - 1)
                    if later(s, RING):
                        dve.wait_ge(x_loaded[u], chunk_load(s - RING, u))
                    else:
                        dve.wait_ge(x_first[s], 16)
                    for k in range(TPC):
                        last = nc.vector.bn_stats(bn[:, b, k, :], X[:, bass.ds(s * TPC + k, 1), :])
                    last.then_inc(bn_ready, 1)
                if at(t, -3):
                    dve.wait_ge(w1H_ready, 1)
                    nc.vector.tensor_tensor(w1L[:], w1raw[:], w1H[:].bitcast(f32), ALU.subtract)\
                        .then_inc(w1_ready, 1)
                    dve.wait_ge(w3H_ready, 1)
                    nc.vector.tensor_tensor(V[:, KT:KT + FC, 1, :], w3raw[:], V[:, KT:KT + FC, 0, :].bitcast(f32),
                                            ALU.subtract).then_inc(w3_ready, 1)
                if inside(t + 2, CHUNKS):
                    s, b = t + 2, u % 2
                    dve.wait_ge(hH_ready, s + 1)
                    nc.vector.scalar_tensor_tensor(out=hL[:, b], in0=hT[b], scalar=0.0, in1=hH[:, b].bitcast(f32),
                                                   op0=ALU.max, op1=ALU.subtract).then_inc(h_ready, 1)
                if inside(t + 1, CHUNKS):
                    s, b = t + 1, (u + 1) % 2
                    vt = V[:, bass.ds(s * TPC, TPC), :, :]
                    dve.wait_ge(vH_ready, s + 1)
                    nc.vector.tensor_tensor(vt[:, :, 1, :], vf[:, b], vt[:, :, 0, :].bitcast(f32), ALU.subtract)\
                        .then_inc(v_ready, 1)
                if at(t, -2):
                    split_xg_low(0)
                if inside(t + LEAD, CHUNKS):
                    dve.wait_ge(bn_ready, t + LEAD + 1)
                if inside(t + 2, CHUNKS):
                    split_low(t + 2, (u + 2) % RING)
                if inside(t + LEAD, CHUNKS):
                    s, b = t + LEAD, u % 2
                    for k in range(TPC):
                        last = nc.vector.bn_aggr(mv[:, b, k, :], bn[:, b, k, :])
                    last.then_inc(mv_ready, 1)
                if inside(t + 2, CHUNKS):
                    s, b = t + 2, u % 2
                    slot = (u + 2) % RING
                    dve.wait_ge(w2_loaded[slot], chunk_load(s, slot))
                    dve.wait_ge(vP_ready, s + 1)
                    if later(s, 2):
                        dve.wait_ge(v_ready, s - 1)
                    nc.vector.tensor_tensor(vf[:, b], vP[b], w2s[:, slot], ALU.add).then_inc(vf_ready, 1)
                if inside(t + LEAD, CHUNKS):
                    s, b = t + LEAD, u % 2
                    dve.wait_ge(sd_ready, s + 1)
                    nc.vector.reciprocal(r0[:, b], sd[:, b]).then_inc(r0_ready, 1)

            def group(g, par):
                split_xg_low(g)
                with dve.Fori(0, ITER) as i:
                    for u in range(RING):
                        split_low(g * CHUNKS + i * RING + u, u)
                    evacuate(g - 1, 1 - par, i)

            steps(dve, step)
            groups(dve, group)
            for j in range(TPG):
                evacuate(GROUPS - 1, 1, j)

        @block.tensor
        def _(pe):
            def products(bank, high, low, v, first, last):
                nc.tensor.matmul(acc[:, bank], high, v, start=first, stop=False)
                return nc.tensor.matmul(acc[:, bank, 0, :], low, v[:, 0, :], start=False, stop=last)

            def sum_xg(g, par):
                pe.wait_ge(xg_ready, g + 1)
                for j in range(TPG):
                    rows = slice(j * P, (j + 1) * P)
                    for f in range(FC):
                        last = products(par * TPG + j, xgH[:, f, rows], xgL[:, f, rows], V[:, KT + f], f == 0, False)
                last.then_inc(xg_used, 1)

            def sum_tiles(c, slot, par, tiles):
                for j in tiles:
                    rows = slice(j * P, (j + 1) * P)
                    for k in range(TPC):
                        v = V[:, bass.ds(c * TPC + k, 1), :, :].rearrange("p a h f -> p (a h) f")
                        last = products(par * TPG + j, aH[:, slot, k, rows], aL[:, slot, k, rows], v, False,
                                        at(c, CHUNKS - 1) and k == TPC - 1)
                    last.then_inc(tile_summed, 1)

            def step(t, u):
                if inside(t + 2, CHUNKS):
                    s, b = t + 2, u % 2
                    pe.wait_ge(xn_ready, s + 1)
                    if at(s, 0):
                        pe.wait_ge(ident_ready, 1)
                    if later(s, 2):
                        pe.wait_ge(h_ready, s - 1)
                    for f in range(FC):
                        for k in range(TPC):
                            last = nc.tensor.transpose(hT[b][:, f, k * P:(k + 1) * P],
                                                       xn[:, b, k, f * P:(f + 1) * P], ident[:])
                    last.then_inc(hT_ready, 1)
                if at(t, -1):
                    pe.wait_ge(w3_ready, 1)
                    sum_xg(0, 0)
                if inside(t, CHUNKS):
                    pe.wait_ge(v_ready, t + 1)
                    pe.wait_ge(a_ready, t + 1)
                    sum_tiles(t, u, 0, range(0, TPG - 1))
                if inside(t + 2, CHUNKS):
                    s, b = t + 2, u % 2
                    pe.wait_ge(h_ready, s + 1)
                    if at(s, 0):
                        pe.wait_ge(w1_ready, 1)
                    if later(s, 2):
                        pe.wait_ge(vf_ready, s - 1)
                    for k in range(TPC):
                        nodes = slice(k * P, (k + 1) * P)
                        for f in range(FC):
                            h_high, h_low = hH[:, b, f, nodes], hL[:, b, f, nodes]
                            nc.tensor.matmul(vP[b][:, k], h_high, w1H[:, f, :], start=f == 0, stop=False)
                            nc.tensor.matmul(vP[b][:, k], h_high, w1L[:, f, :], start=False, stop=False)
                            last = nc.tensor.matmul(vP[b][:, k], h_low, w1H[:, f, :], start=False,
                                                    stop=f == FC - 1)
                    last.then_inc(vP_ready, 1)
                if inside(t, CHUNKS):
                    sum_tiles(t, u, 0, range(TPG - 1, TPG))

            def sum_chunk(n, c, slot, par):
                pe.wait_ge(a_ready, n + 1)
                sum_tiles(c, slot, par, range(TPG))

            def group(g, par):
                if later(g, 2):
                    pe.wait_ge(evacuated, g * TPG - TPG)
                sum_xg(g, par)
                with pe.Fori(0, ITER - 1) as i:
                    for u in range(RING):
                        sum_chunk(g * CHUNKS + i * RING + u, i * RING + u, u, par)
                for c in range(CHUNKS - RING, CHUNKS):
                    sum_chunk(g * CHUNKS + c, c, c % RING, par)

            steps(pe, step)
            groups(pe, group)


def kernel(x, adj, L0_gnn_x, L0_gnn_weight, L0_gnn_bias):
    import numpy as np
    import concourse.bacc as bacc
    from concourse.bass_utils import run_bass_kernel_spmd

    w = np.asarray(L0_gnn_weight)
    tiles = lambda a: np.ascontiguousarray(np.asarray(a).reshape(-1, P, F).transpose(1, 0, 2))
    arrays = {
        "x": tiles(x),
        "adj": np.ascontiguousarray(
            np.asarray(adj).reshape(GROUPS, ROWS, CHUNKS, TPC, P).transpose(0, 2, 4, 3, 1)),
        "xg": np.ascontiguousarray(np.asarray(L0_gnn_x).reshape(GROUPS, ROWS, FC, P).transpose(0, 3, 2, 1)),
        "w1": tiles(w[:F]),
        "w2": tiles(w[F:F + N]),
        "w3": tiles(w[F + N:]),
        "bias": np.ascontiguousarray(np.asarray(L0_gnn_bias).reshape(1, F)),
    }
    nc = bacc.Bacc("TRN2", target_bir_lowering=False, num_devices=1)
    args = [nc.dram_tensor(name, a.shape, mybir.dt.from_np(a.dtype), kind="ExternalInput").ap()
            for name, a in arrays.items()]
    out = nc.dram_tensor("out", (GROUPS, P, TPG, F), mybir.dt.float32, kind="ExternalOutput").ap()
    build(nc, *args, out)
    r = run_bass_kernel_spmd(nc, [arrays], core_ids=[0])
    return r.results[0]["out"].transpose(0, 2, 1, 3).reshape(N, F)
```

```python
import concourse.bass as bass
from concourse import mybir
from contextlib import ExitStack


P = 128
N = 4096
F = 256
FC = F // P
KT = N // P
TPC = 2
CHUNKS = KT // TPC
TPG = 4
ROWS = TPG * P
GROUPS = N // ROWS
RING = 4
ITER = CHUNKS // RING
EPS = 1e-5
WARMUP = 9
assert ITER == TPG


def build(nc, x, adj, xg, w1, w2, w3, bias, out):
    f32 = mybir.dt.float32
    f32r = mybir.dt.float32r
    ALU = mybir.AluOpType
    ACT = mybir.ActivationFunctionType

    ctx = ExitStack()
    with ctx:
        def sb(name, shape, dt=f32):
            return ctx.enter_context(nc.sbuf_tensor(name, shape, dt))

        def sem(name):
            return ctx.enter_context(nc.semaphore(name))

        V = sb("V", [P, KT + FC, 2, F], f32r)
        X = sb("X", [P, KT, F])
        raw = sb("raw", [P, RING, TPC, ROWS])
        aH = sb("aH", [P, RING, TPC, ROWS], f32r)
        aL = sb("aL", [P, RING, TPC, ROWS], f32r)
        xgraw = sb("xgraw", [P, FC, ROWS])
        xgH = sb("xgH", [P, FC, ROWS], f32r)
        xgL = sb("xgL", [P, FC, ROWS], f32r)
        w2s = sb("w2s", [P, RING, TPC, F])
        w1raw = sb("w1raw", [P, FC, F])
        w3raw = sb("w3raw", [P, FC, F])
        w1H = sb("w1H", [P, FC, F], f32r)
        w1L = sb("w1L", [P, FC, F], f32r)
        bias_all = sb("bias_all", [P, F])
        ident = sb("ident", [P, P])
        eps = sb("eps", [P, 1])
        warm = sb("warm", [P, 1])
        bn = sb("bn", [P, 2, TPC, 6])
        mv = sb("mv", [P, 2, TPC, 2])
        sd = sb("sd", [P, 2, TPC])
        r0 = sb("r0", [P, 2, TPC])
        nwt = sb("nwt", [P, 2, 5, TPC])
        rstd = sb("rstd", [P, 2, TPC])
        nmr = sb("nmr", [P, 2, TPC])
        xn = sb("xn", [P, 2, TPC, F])
        hH = sb("hH", [P, 2, FC, TPC * P], f32r)
        hL = sb("hL", [P, 2, FC, TPC * P], f32r)
        vf = sb("vf", [P, 2, TPC, F])
        outs = sb("outs", [P, TPG, F])

        acc = ctx.enter_context(nc.psum_tensor("acc", [P, 2 * TPG, 2, F], f32))
        hT = [acc[:, 4 + b, :, :] for b in range(2)]
        vP = [acc[:, 6 + b, :, :] for b in range(2)]

        w1_loaded, w3_loaded = sem("w1_loaded"), sem("w3_loaded")
        bias_loaded = sem("bias_loaded")
        x_first = [sem(f"x_first{i}") for i in range(RING)]
        x_loaded = [sem(f"x_loaded{i}") for i in range(RING)]
        w2_loaded = [sem(f"w2_loaded{i}") for i in range(RING)]
        adj_loaded = [sem(f"adj_loaded{i}") for i in range(RING)]
        xg_loaded = sem("xg_loaded")
        ident_zero, ident_ready = sem("ident_zero"), sem("ident_ready")
        warmed = sem("warmed")
        bn_ready, mv_ready = sem("bn_ready"), sem("mv_ready")
        sd_ready, r0_ready = sem("sd_ready"), sem("r0_ready")
        newton, rstd_ready = sem("newton"), sem("rstd_ready")
        xn_ready, hT_ready = sem("xn_ready"), sem("hT_ready")
        hH_ready, h_ready = sem("hH_ready"), sem("h_ready")
        vP_ready, vf_ready = sem("vP_ready"), sem("vf_ready")
        vH_ready, v_ready = sem("vH_ready"), sem("v_ready")
        w1H_ready, w1_ready = sem("w1H_ready"), sem("w1_ready")
        w3H_ready, w3_ready = sem("w3H_ready"), sem("w3_ready")
        xgH_ready, xg_ready, xg_used = sem("xgH_ready"), sem("xg_ready"), sem("xg_used")
        aH_ready, a_ready = sem("aH_ready"), sem("a_ready")
        tile_summed = sem("tile_summed")
        biased, half_added, evacuated = sem("biased"), sem("half_added"), sem("evacuated")
        out_stored, tail_stored = sem("out_stored"), sem("tail_stored")

        block = ctx.enter_context(nc.Block())

        def inside(i, last):
            return not isinstance(i, int) or 0 <= i < last

        def later(i, first):
            return not isinstance(i, int) or i >= first

        def early(i):
            return isinstance(i, int) and i < 0

        def at(i, step):
            return isinstance(i, int) and i == step

        def chunk_load(n, slot):
            return (n + (RING - slot)) * (16 // RING)

        LEAD = 4

        def steps(eng, step):
            for t in range(-LEAD, 0):
                step(t, t % RING)
            with eng.Fori(0, ITER - 1) as i:
                for u in range(RING):
                    step(i * RING + u, u)
            for t in range(CHUNKS - RING, CHUNKS):
                step(t, t % RING)

        def groups(eng, group):
            group(1, 1)
            with eng.Fori(0, (GROUPS - 2) // 2) as pair:
                group(pair * 2 + 2, 0)
                group(pair * 2 + 3, 1)

        @block.sync
        def _(sp):
            def load_adj(g, c, slot):
                sp.dma_start(raw[:, slot], adj[g, c]).then_inc(adj_loaded[slot], 16)

            def load_w2(s, slot):
                sp.dma_start(w2s[:, slot], w2[:, bass.ds(s * TPC, TPC), :]).then_inc(w2_loaded[slot], 16)

            def load_first_x(s):
                sp.dma_start(X[:, s * TPC:(s + 1) * TPC, :], x[:, s * TPC:(s + 1) * TPC, :]).then_inc(x_first[s], 16)

            load_first_x(0)
            sp.dma_start(w3raw[:], w3).then_inc(w3_loaded, 16)
            sp.dma_start(xgraw[:], xg[0]).then_inc(xg_loaded, 16)
            load_first_x(1)
            sp.dma_start(w1raw[:], w1).then_inc(w1_loaded, 16)
            load_adj(0, 0, 0)
            load_w2(0, 0)
            load_first_x(2)
            load_adj(0, 1, 1)
            load_w2(1, 1)
            load_first_x(3)
            for s in range(2, RING):
                load_adj(0, s, s)
                load_w2(s, s)
            sp.dma_start(bias_all[:], bias.to_broadcast([P, F])).then_inc(bias_loaded, 16)
            with sp.Fori(1, ITER) as i:
                for u in range(RING):
                    c = i * RING + u
                    sp.wait_ge(vf_ready, c - (RING - 1))
                    load_w2(c, u)
                    sp.wait_ge(a_ready, c - (RING - 1))
                    load_adj(0, c, u)
            with sp.Fori(1, GROUPS) as g:
                sp.wait_ge(xg_ready, g)
                sp.dma_start(xgraw[:], xg[g]).then_inc(xg_loaded, 16)
                with sp.Fori(0, ITER) as i:
                    for u in range(RING):
                        sp.wait_ge(a_ready, g * CHUNKS + i * RING + (u - (RING - 1)))
                        load_adj(g, i * RING + u, u)
            for j in range(TPG):
                sp.wait_ge(evacuated, (GROUPS - 1) * TPG + j + 1)
                sp.dma_start(out[GROUPS - 1, :, j, :], outs[:, j, :]).then_inc(tail_stored, 16)
            sp.wait_ge(tail_stored, 16 * TPG)

        @block.gpsimd
        def _(pool):
            nc.gpsimd.memset(ident[:], 0.0).then_inc(ident_zero, 1)
            pool.wait_ge(ident_zero, 1)
            nc.gpsimd.affine_select(out=ident[:], in_=ident[:], compare_op=ALU.not_equal, fill=1.0, base=0,
                                    pattern=[[-1, P]], channel_multiplier=1).then_inc(ident_ready, 1)

            def step(t, u):
                s = t + LEAD
                b = u % 2
                if not inside(s, CHUNKS):
                    return
                var, mean = mv[:, b, :, 1], mv[:, b, :, 0]
                half, r15, negmean, sq, cube = (nwt[:, b, k, :] for k in range(5))
                r = r0[:, b]
                pool.wait_ge(r0_ready, s + 1)
                if later(s, 2):
                    pool.wait_ge(xn_ready, s - 1)
                nc.gpsimd.tensor_tensor(sq, r, r, ALU.mult).then_inc(newton, 1)
                nc.gpsimd.tensor_scalar(half, var, EPS, -0.5, ALU.add, ALU.mult).then_inc(newton, 1)
                pool.wait_ge(newton, s * 7 + 2)
                nc.gpsimd.tensor_tensor(sq, sq, half, ALU.mult).then_inc(newton, 1)
                nc.gpsimd.tensor_scalar(r15, r, 1.5, 1.0, ALU.mult, ALU.mult).then_inc(newton, 1)
                pool.wait_ge(newton, s * 7 + 3)
                nc.gpsimd.tensor_tensor(cube, sq, r, ALU.mult).then_inc(newton, 1)
                nc.gpsimd.tensor_scalar(negmean, mean, -1.0, 1.0, ALU.mult, ALU.mult).then_inc(newton, 1)
                pool.wait_ge(newton, s * 7 + 5)
                nc.gpsimd.tensor_tensor(rstd[:, b], cube, r15, ALU.add).then_inc(newton, 1)
                pool.wait_ge(newton, s * 7 + 7)
                nc.gpsimd.tensor_tensor(nmr[:, b], negmean, rstd[:, b], ALU.mult).then_inc(rstd_ready, 1)
                if inside(s + RING, CHUNKS):
                    load_x(s + RING, u)

            def load_x(s, slot):
                pool.dma_start(X[:, bass.ds(s * TPC, TPC), :], x[:, bass.ds(s * TPC, TPC), :])\
                    .then_inc(x_loaded[slot], 16)

            for t in range(-LEAD, 0):
                step(t, t % RING)
            with pool.Fori(0, ITER - 2) as i:
                for u in range(RING):
                    step(i * RING + u, u)
            for t in range(CHUNKS - 2 * RING, CHUNKS - RING):
                step(t, t % RING)

            pool.wait_ge(xn_ready, CHUNKS)
            pool.wait_ge(bias_loaded, 16)
            with pool.Fori(0, GROUPS - 1) as g:
                with pool.Fori(0, TPG) as j:
                    tile = X[:, bass.ds(g * TPG + j, 1), :]
                    nc.gpsimd.tensor_tensor(tile, tile, bias_all[:].rearrange("p (a f) -> p a f", a=1),
                                            ALU.add).then_inc(biased, 1)
                pool.wait_ge(evacuated, g * TPG + TPG)
                pool.dma_start(out[g], outs[:]).then_inc(out_stored, 16)
            for j in range(TPG):
                tile = X[:, (GROUPS - 1) * TPG + j, :]
                nc.gpsimd.tensor_tensor(tile, tile, bias_all[:], ALU.add).then_inc(biased, 1)
            pool.wait_ge(out_stored, 16 * (GROUPS - 1))

        @block.scalar
        def _(act):
            def split_high(n, slot):
                act.wait_ge(adj_loaded[slot], chunk_load(n, slot))
                if later(n, RING):
                    act.wait_ge(tile_summed, n * TPG - ((RING - 1) * TPG - 1))
                nc.scalar.activation(aH[:, slot], raw[:, slot], ACT.Copy).then_inc(aH_ready, 1)

            def split_xg_high(g):
                act.wait_ge(xg_loaded, g * 16 + 16)
                if later(g, 1):
                    act.wait_ge(xg_used, g)
                nc.scalar.activation(xgH[:], xgraw[:], ACT.Copy).then_inc(xgH_ready, 1)

            def step(t, u):
                if at(t, -LEAD):
                    act.wait_ge(w3_loaded, 16)
                    nc.scalar.activation(V[:, KT:KT + FC, 0, :], w3raw[:], ACT.Copy).then_inc(w3H_ready, 1)
                    deviation(t + LEAD, u % 2)
                    split_xg_high(0)
                if at(t, -LEAD + 1):
                    act.wait_ge(w1_loaded, 16)
                    nc.scalar.activation(w1H[:], w1raw[:], ACT.Copy).then_inc(w1H_ready, 1)
                if inside(t + 2, CHUNKS):
                    s, b = t + 2, u % 2
                    act.wait_ge(hT_ready, s + 1)
                    if later(s, 2):
                        act.wait_ge(vP_ready, s - 1)
                    nc.scalar.activation(hH[:, b], hT[b], ACT.Relu).then_inc(hH_ready, 1)
                if inside(t + 1, CHUNKS):
                    s, b = t + 1, (u + 1) % 2
                    act.wait_ge(vf_ready, s + 1)
                    nc.scalar.activation(V[:, bass.ds(s * TPC, TPC), 0, :], vf[:, b], ACT.Copy)\
                        .then_inc(vH_ready, 1)
                if inside(t + 3, CHUNKS):
                    if early(t):
                        if at(t, -2):
                            split_high(0, 0)
                        normalise(t + 3, (u + 3) % 2)
                        deviation(t + LEAD, u % 2)
                        if not at(t, -3):
                            split_high(t + 3, (u + 3) % RING)
                    else:
                        split_high(t + 3, (u + 3) % RING)
                        normalise(t + 3, (u + 3) % 2)
                if inside(t + LEAD, CHUNKS) and not early(t):
                    deviation(t + LEAD, u % 2)

            def normalise(s, b):
                act.wait_ge(rstd_ready, s + 1)
                if later(s, 2):
                    act.wait_ge(hT_ready, s - 1)
                for k in range(TPC):
                    last = nc.scalar.activation(xn[:, b, k, :], X[:, bass.ds(s * TPC + k, 1), :], ACT.Identity,
                                                bias=nmr[:, b, k:k + 1], scale=rstd[:, b, k:k + 1])
                last.then_inc(xn_ready, 1)

            def deviation(s, b):
                act.wait_ge(mv_ready, s + 1)
                if later(s, 2):
                    act.wait_ge(r0_ready, s - 1)
                nc.scalar.activation(sd[:, b], mv[:, b, :, 1], ACT.Sqrt, bias=eps[:]).then_inc(sd_ready, 1)

            def group(g, par):
                split_xg_high(g)
                with act.Fori(0, ITER) as i:
                    for u in range(RING):
                        split_high(g * CHUNKS + i * RING + u, u)

            act.wait_ge(tile_summed, 1)
            nc.scalar.activation(warm[:], eps[:], ACT.Sqrt, bias=eps[:]).then_inc(warmed, 1)
            steps(act, step)
            groups(act, group)

        @block.vector
        def _(dve):
            nc.vector.memset(eps[:], EPS).then_inc(tile_summed, 1)

            def split_low(n, slot):
                dve.wait_ge(aH_ready, n + 1)
                nc.vector.tensor_tensor(aL[:, slot], raw[:, slot], aH[:, slot].bitcast(f32), ALU.subtract)\
                    .then_inc(a_ready, 1)

            def split_xg_low(g):
                dve.wait_ge(xgH_ready, g + 1)
                nc.vector.tensor_tensor(xgL[:], xgraw[:], xgH[:].bitcast(f32), ALU.subtract).then_inc(xg_ready, 1)

            def evacuate(e, par, j):
                tile = X[:, bass.ds(e * TPG + j, 1), :]
                o = outs[:, bass.ds(j, 1), :]
                if later(e, 1):
                    dve.wait_ge(out_stored, e * 16)
                dve.wait_ge(biased, e * TPG + j + 1)
                dve.wait_ge(tile_summed, e * (CHUNKS * TPG) + ((CHUNKS - 1) * TPG + 2) + j)
                nc.vector.tensor_tensor(o, acc[:, bass.ds(par * TPG + j, 1), 1, :], tile, ALU.add)\
                    .then_inc(half_added, 1)
                dve.wait_ge(half_added, e * TPG + j + 1)
                nc.vector.tensor_tensor(o, acc[:, bass.ds(par * TPG + j, 1), 0, :], o, ALU.add)\
                    .then_inc(evacuated, 1)

            def h_low(s, b):
                dve.wait_ge(hH_ready, s + 1)
                nc.vector.scalar_tensor_tensor(out=hL[:, b], in0=hT[b], scalar=0.0, in1=hH[:, b].bitcast(f32),
                                               op0=ALU.max, op1=ALU.subtract).then_inc(h_ready, 1)

            def step(t, u):
                if inside(t + 2, CHUNKS) and early(t):
                    h_low(t + 2, u % 2)
                if inside(t + LEAD, CHUNKS):
                    s, b = t + LEAD, u % 2
                    if later(s, 2):
                        dve.wait_ge(rstd_ready, s - 1)
                    if later(s, RING):
                        dve.wait_ge(x_loaded[u], chunk_load(s - RING, u))
                    else:
                        dve.wait_ge(x_first[s], 16)
                    for k in range(TPC):
                        last = nc.vector.bn_stats(bn[:, b, k, :], X[:, bass.ds(s * TPC + k, 1), :])
                    last.then_inc(bn_ready, 1)
                    if early(t):
                        dve.wait_ge(bn_ready, s + 1)
                        aggregate(s, b)
                if at(t, -LEAD):
                    dve.wait_ge(w3H_ready, 1)
                    nc.vector.tensor_tensor(V[:, KT:KT + FC, 1, :], w3raw[:], V[:, KT:KT + FC, 0, :].bitcast(f32),
                                            ALU.subtract).then_inc(w3_ready, 1)
                    invert(t + LEAD, u % 2)
                    split_xg_low(0)
                if at(t, -LEAD + 1):
                    dve.wait_ge(w1H_ready, 1)
                    nc.vector.tensor_tensor(w1L[:], w1raw[:], w1H[:].bitcast(f32), ALU.subtract)\
                        .then_inc(w1_ready, 1)
                if inside(t + 2, CHUNKS) and not early(t):
                    h_low(t + 2, u % 2)
                if inside(t + 1, CHUNKS):
                    s, b = t + 1, (u + 1) % 2
                    vt = V[:, bass.ds(s * TPC, TPC), :, :]
                    dve.wait_ge(vH_ready, s + 1)
                    nc.vector.tensor_tensor(vt[:, :, 1, :], vf[:, b], vt[:, :, 0, :].bitcast(f32), ALU.subtract)\
                        .then_inc(v_ready, 1)
                if inside(t + LEAD, CHUNKS) and not early(t):
                    dve.wait_ge(bn_ready, t + LEAD + 1)
                if inside(t + 2, CHUNKS):
                    split_low(t + 2, (u + 2) % RING)
                if inside(t + LEAD, CHUNKS) and not early(t):
                    aggregate(t + LEAD, u % 2)
                if inside(t + 2, CHUNKS):
                    s, b = t + 2, u % 2
                    slot = (u + 2) % RING
                    dve.wait_ge(w2_loaded[slot], chunk_load(s, slot))
                    dve.wait_ge(vP_ready, s + 1)
                    if later(s, 2):
                        dve.wait_ge(v_ready, s - 1)
                    nc.vector.tensor_tensor(vf[:, b], vP[b], w2s[:, slot], ALU.add).then_inc(vf_ready, 1)
                if inside(t + LEAD, CHUNKS) and not at(t, -LEAD):
                    invert(t + LEAD, u % 2)

            def aggregate(s, b):
                for k in range(TPC):
                    last = nc.vector.bn_aggr(mv[:, b, k, :], bn[:, b, k, :])
                last.then_inc(mv_ready, 1)

            def invert(s, b):
                dve.wait_ge(sd_ready, s + 1)
                nc.vector.reciprocal(r0[:, b], sd[:, b]).then_inc(r0_ready, 1)

            def group(g, par):
                split_xg_low(g)
                with dve.Fori(0, ITER) as i:
                    for u in range(RING):
                        split_low(g * CHUNKS + i * RING + u, u)
                    evacuate(g - 1, 1 - par, i)

            steps(dve, step)
            groups(dve, group)
            for j in range(TPG):
                evacuate(GROUPS - 1, 1, j)

        @block.tensor
        def _(pe):
            def products(bank, high, low, v, first, last):
                nc.tensor.matmul(acc[:, bank], high, v, start=first, stop=False)
                return nc.tensor.matmul(acc[:, bank, 0, :], low, v[:, 0, :], start=False, stop=last)

            def sum_xg(g, par, tiles=range(TPG)):
                if tiles[0] == 0:
                    pe.wait_ge(xg_ready, g + 1)
                for j in tiles:
                    rows = slice(j * P, (j + 1) * P)
                    for f in range(FC):
                        last = products(par * TPG + j, xgH[:, f, rows], xgL[:, f, rows], V[:, KT + f], f == 0, False)
                if tiles[-1] == TPG - 1:
                    last.then_inc(xg_used, 1)

            def sum_tiles(c, slot, par, tiles):
                for j in tiles:
                    rows = slice(j * P, (j + 1) * P)
                    for k in range(TPC):
                        v = V[:, bass.ds(c * TPC + k, 1), :, :].rearrange("p a h f -> p (a h) f")
                        last = products(par * TPG + j, aH[:, slot, k, rows], aL[:, slot, k, rows], v, False,
                                        at(c, CHUNKS - 1) and k == TPC - 1)
                    last.then_inc(tile_summed, 1)

            def step(t, u):
                if inside(t + 2, CHUNKS):
                    s, b = t + 2, u % 2
                    pe.wait_ge(xn_ready, s + 1)
                    if later(s, 2):
                        pe.wait_ge(h_ready, s - 1)
                    for f in range(FC):
                        for k in range(TPC):
                            last = nc.tensor.transpose(hT[b][:, f, k * P:(k + 1) * P],
                                                       xn[:, b, k, f * P:(f + 1) * P], ident[:])
                    last.then_inc(hT_ready, 1)
                if at(t, -2):
                    pe.wait_ge(w3_ready, 1)
                    sum_xg(0, 0, range(0, 2))
                if at(t, -1):
                    sum_xg(0, 0, range(2, 4))
                if inside(t, CHUNKS):
                    pe.wait_ge(v_ready, t + 1)
                    pe.wait_ge(a_ready, t + 1)
                    sum_tiles(t, u, 0, range(0, TPG - 1))
                if inside(t + 2, CHUNKS):
                    s, b = t + 2, u % 2
                    pe.wait_ge(h_ready, s + 1)
                    if at(s, 0):
                        pe.wait_ge(w1_ready, 1)
                    if later(s, 2):
                        pe.wait_ge(vf_ready, s - 1)
                    for k in range(TPC):
                        nodes = slice(k * P, (k + 1) * P)
                        for f in range(FC):
                            h_high, h_low = hH[:, b, f, nodes], hL[:, b, f, nodes]
                            nc.tensor.matmul(vP[b][:, k], h_high, w1H[:, f, :], start=f == 0, stop=False)
                            nc.tensor.matmul(vP[b][:, k], h_high, w1L[:, f, :], start=False, stop=False)
                            last = nc.tensor.matmul(vP[b][:, k], h_low, w1H[:, f, :], start=False,
                                                    stop=f == FC - 1)
                    last.then_inc(vP_ready, 1)
                if inside(t, CHUNKS):
                    sum_tiles(t, u, 0, range(TPG - 1, TPG))

            def sum_chunk(n, c, slot, par):
                pe.wait_ge(a_ready, n + 1)
                sum_tiles(c, slot, par, range(TPG))

            def group(g, par):
                if later(g, 2):
                    pe.wait_ge(evacuated, g * TPG - TPG)
                sum_xg(g, par)
                with pe.Fori(0, ITER - 1) as i:
                    for u in range(RING):
                        sum_chunk(g * CHUNKS + i * RING + u, i * RING + u, u, par)
                for c in range(CHUNKS - RING, CHUNKS):
                    sum_chunk(g * CHUNKS + c, c, c % RING, par)

            pe.wait_ge(ident_ready, 1)
            with pe.Fori(0, WARMUP):
                for b in range(2):
                    nc.tensor.matmul(vP[b][:, 0, 0:P], ident[:], ident[:], start=True, stop=True)
            steps(pe, step)
            groups(pe, group)


def kernel(x, adj, L0_gnn_x, L0_gnn_weight, L0_gnn_bias):
    import numpy as np
    import concourse.bacc as bacc
    from concourse.bass_utils import run_bass_kernel_spmd

    w = np.asarray(L0_gnn_weight)
    tiles = lambda a: np.ascontiguousarray(np.asarray(a).reshape(-1, P, F).transpose(1, 0, 2))
    arrays = {
        "x": tiles(x),
        "adj": np.ascontiguousarray(
            np.asarray(adj).reshape(GROUPS, ROWS, CHUNKS, TPC, P).transpose(0, 2, 4, 3, 1)),
        "xg": np.ascontiguousarray(np.asarray(L0_gnn_x).reshape(GROUPS, ROWS, FC, P).transpose(0, 3, 2, 1)),
        "w1": tiles(w[:F]),
        "w2": tiles(w[F:F + N]),
        "w3": tiles(w[F + N:]),
        "bias": np.ascontiguousarray(np.asarray(L0_gnn_bias).reshape(1, F)),
    }
    nc = bacc.Bacc("TRN2", target_bir_lowering=False, num_devices=1)
    args = [nc.dram_tensor(name, a.shape, mybir.dt.from_np(a.dtype), kind="ExternalInput").ap()
            for name, a in arrays.items()]
    out = nc.dram_tensor("out", (GROUPS, P, TPG, F), mybir.dt.float32, kind="ExternalOutput").ap()
    build(nc, *args, out)
    r = run_bass_kernel_spmd(nc, [arrays], core_ids=[0])
    return r.results[0]["out"].transpose(0, 2, 1, 3).reshape(N, F)
```
